# Optimizing a Trainium2 kernel written in Bass

```python
import numpy as np
import jax
import jax.numpy as jnp

def _softmax(x, axis=-1):
    return jax.nn.softmax(x, axis=axis)

def _gelu(x):
    return jax.nn.gelu(x, approximate=True)

def _silu(x):
    return jax.nn.silu(x)

def _sigmoid(x):
    return jax.nn.sigmoid(x)

def _layernorm(x, axis=-1, eps=1e-05):
    m = jnp.mean(x, axis=axis, keepdims=True)
    v = jnp.var(x, axis=axis, keepdims=True)
    return (x - m) / jnp.sqrt(v + eps)

def _scatter_add(tgt, idx, src, axis=0):
    return tgt.at[idx].add(src)

def _segment_sum(src, seg, n):
    return jax.ops.segment_sum(src, seg, n)
kernel_name = 'mk_adj_resnorm_d1_adj_r2_f43521'

def setup_inputs(seed: int=0):
    np.random.seed(seed)
    _w = jnp.asarray

    def _rec_inputs():
        import jax
        import jax.numpy as jnp
        _gk = jax.random.key(seed)
        x = -8.776e-05 + 1 * jax.random.normal(jax.random.fold_in(_gk, 1), (10000, 128), jnp.float32)
        _w = (1.0 + jnp.arange(10000, dtype=jnp.float32)) ** (-0.5)
        _w = _w / _w.mean()
        _pij = jnp.clip(0.0008 * _w[:, None] * _w[None, :], 0.0, 1.0)
        _a = jax.random.uniform(jax.random.fold_in(_gk, 2), (10000, 10000)) < _pij
        _a = jnp.logical_or(_a, jnp.eye(10000, dtype=bool))
        _af = _a.astype(jnp.float32)
        _af = _af * jax.random.uniform(jax.random.fold_in(_gk, 3), (10000, 10000), jnp.float32, 0.05, 1)
        adj = _af
        return (x, adj)
    x, adj = _rec_inputs()

    def _L0_gnn_setup():
        import jax, jax.numpy as jnp
        import numpy as np
        N_USER = 10000
        N_ITEM = 10000
        HID = 128
        key = jax.random.key(seed)
        k1, k2, k3, k4, k5, k6, k7 = jax.random.split(key, 7)
        scale = 1.0 / np.sqrt(HID)
        return {'user_feat': jax.random.normal(k1, (N_USER, HID), dtype=jnp.float32), 'item_feat': jax.random.normal(k2, (N_ITEM, HID), dtype=jnp.float32), 'adj': jax.random.uniform(k3, (N_USER, N_ITEM), dtype=jnp.float32), 'W_item': jax.random.uniform(k4, (HID, HID), dtype=jnp.float32, minval=-scale, maxval=scale), 'b_item': jax.random.uniform(k5, (HID,), dtype=jnp.float32, minval=-scale, maxval=scale), 'W_user': jax.random.uniform(k6, (HID, HID), dtype=jnp.float32, minval=-scale, maxval=scale), 'b_user': jax.random.uniform(k7, (HID,), dtype=jnp.float32, minval=-scale, maxval=scale)}
    _L0_gnn_all = _L0_gnn_setup()
    _L0_gnn_in = {k: v for k, v in _L0_gnn_all.items() if k in ('item_feat', 'W_item', 'b_item', 'W_user', 'b_user')}
    del _L0_gnn_all
    return {'x': x, 'adj': adj, 'L0_gnn_item_feat': _L0_gnn_in['item_feat'], 'L0_gnn_W_item': _L0_gnn_in['W_item'], 'L0_gnn_b_item': _L0_gnn_in['b_item'], 'L0_gnn_W_user': _L0_gnn_in['W_user'], 'L0_gnn_b_user': _L0_gnn_in['b_user']}

def reference(x, adj, L0_gnn_item_feat, L0_gnn_W_item, L0_gnn_b_item, L0_gnn_W_user, L0_gnn_b_user):
    import jax
    import jax.numpy as jnp

    def _L0_gnn_ref(user_feat, item_feat, adj, W_item, b_item, W_user, b_user):
        import jax, jax.numpy as jnp
        import numpy as np
        N_USER = 10000
        N_ITEM = 10000
        HID = 128
        h = item_feat @ W_item.T + b_item
        b = user_feat @ W_user.T + b_user
        return jax.nn.relu(adj @ h + b)
    x = _layernorm(x + _L0_gnn_ref(x, L0_gnn_item_feat, adj, L0_gnn_W_item, L0_gnn_b_item, L0_gnn_W_user, L0_gnn_b_user), axis=-1)
    return x

_drawn_inputs = setup_inputs


def setup_inputs(seed=0):
    import zlib

    import numpy as np

    out = dict(_drawn_inputs(seed))
    spreads = {}
    factors = {}
    for name, (base, spread) in spreads.items():
        noise = np.random.default_rng([zlib.crc32(name.encode()), seed]).standard_normal(out[name].shape)
        drawn = base * np.exp(spread * noise) if base else spread * noise
        out[name] = jnp.asarray(drawn.astype(out[name].dtype))
    for name, factor in factors.items():
        out[name] = (out[name] * factor).astype(out[name].dtype)
    return out
```

```python
from contextlib import ExitStack

import concourse.bass as bass
from concourse import mybir

FP32 = mybir.dt.float32
ALU = mybir.AluOpType
ACT = mybir.ActivationFunctionType

P = 128
SQ = 32
QUADS = P // SQ
N = 10000
D = 128
EPS = 1e-5

CHUNKS = 6
CB = 13
SEG = CB * SQ
REST = N - CHUNKS * CB * P
LAST_SEG = SEG + REST // QUADS
PAD_SEG = SEG + SQ
BLOCKS = CHUNKS * CB + 1

ROWS = 512
SETS = ROWS // SQ
FULL = N // ROWS
NARROW = -(-(N - FULL * ROWS) // SQ) * SQ
NARROW_AT = N - NARROW
DOUBLE = FULL * ROWS - NARROW_AT
TILES = FULL + 1
PAIRS = (FULL - 1) // 2

RAW = 3
SLOTS = 8
TURNS = -(-BLOCKS // SLOTS) * SLOTS
G = 4
GROUPS = -(-BLOCKS // G)

PE_TURN_OUT = 8
PE_TURN_X = 40
PE_ADD_X = 48
PE_SKEW = PE_TURN_OUT + 1
V_RESIDUAL, V_STATS, V_VAR, V_RSTD, V_NORM = 22, 24, 26, 32, 34
V_SKEW = V_NORM + 1


def chunk_of(k):
    return min(k // CB, CHUNKS - 1)


def seg_of(c):
    return LAST_SEG if c == CHUNKS - 1 else SEG


def col_of(c, a):
    return c * SEG * QUADS + a * seg_of(c)


def segments(rows):
    return [(q, min(P, rows - q * P)) for q in range(-(-rows // P))]


def build(nc, x, adj, item, w_item, b_item, w_user, b_user, out):
    ctx = ExitStack()
    with ctx:
        def sb(name, shape):
            return ctx.enter_context(nc.sbuf_tensor(name, shape, FP32))

        def ps(name, shape):
            return ctx.enter_context(nc.psum_tensor(name, shape, FP32))

        def sem(name):
            return ctx.enter_context(nc.semaphore(name))

        h = sb("h", [P, BLOCKS, D])
        raw = [sb(f"raw{i}", [P, SETS, PAD_SEG]) for i in range(RAW)]
        adjT = sb("adjT", [P, SLOTS, ROWS])
        ident = sb("ident", [P, P])
        w_raw = sb("w_raw", [P, 2, D])
        w_itemT = sb("w_itemT", [P, D])
        w_userT = sb("w_userT", [P, D])
        b_item_row = sb("b_item_row", [P, D])
        b_user_col = sb("b_user_col", [P, 1])
        eps_col = sb("eps_col", [P, 1])
        itemT = sb("itemT", [P, 2, G, P])
        x_nat = sb("x_nat", [P, 2, ROWS // P, D])
        xT = sb("xT", [P, ROWS])
        act_out = sb("act_out", [P, ROWS])
        y = sb("y", [P, ROWS // P, D])
        stats = sb("stats", [P, ROWS // P, 6])
        mv = sb("mv", [P, ROWS // P, 2])
        std = sb("std", [P, ROWS // P])
        rstd = sb("rstd", [P, ROWS // P])
        o = sb("o", [P, 2, ROWS // P, D])

        acc = [ps(f"acc{i}", [P, ROWS]) for i in range(2)]
        ps_t = [ps(f"ps_t{i}", [P, G, P]) for i in range(2)]
        ps_h = [ps(f"ps_h{i}", [P, G, D]) for i in range(2)]
        ps_x = ps("ps_x", [P, ROWS])
        ps_o = ps("ps_o", [P, ROWS // P, D])

        ident_zero = sem("ident_zero")
        ident_ready = sem("ident_ready")
        w_loaded = sem("w_loaded")
        bias_loaded = sem("bias_loaded")
        item_pad = sem("item_pad")
        item_loaded = [sem(f"item_loaded{c}") for c in range(CHUNKS)]
        item_rest_loaded = sem("item_rest_loaded")
        w_turned = sem("w_turned")
        w_ready = sem("w_ready")
        item_turned = sem("item_turned")
        itemT_ready = sem("itemT_ready")
        h_summed = sem("h_summed")
        h_ready = sem("h_ready")
        consts_set = sem("consts_set")
        pad_zeroed = sem("pad_zeroed")
        raw_loaded = [sem(f"raw_loaded{i}") for i in range(RAW)]
        adjT_ready = sem("adjT_ready")
        adjT_used = sem("adjT_used")
        x_loaded = [sem(f"x_loaded{i}") for i in range(2)]
        x_turned = sem("x_turned")
        xT_ready = sem("xT_ready")
        x_done = sem("x_done")
        relu_done = sem("relu_done")
        out_turned = sem("out_turned")
        y_ready = sem("y_ready")
        stats_ready = sem("stats_ready")
        var_ready = sem("var_ready")
        std_ready = sem("std_ready")
        rstd_ready = sem("rstd_ready")
        o_ready = sem("o_ready")
        out_stored = [sem(f"out_stored{i}") for i in range(2)]

        block = ctx.enter_context(nc.Block())

        def wait(eng, s, count):
            if not isinstance(count, int) or count > 0:
                eng.wait_ge(s, count)

        @block.sync
        def _(sp):
            def load_chunk(t, row0, rows, c):
                if c >= RAW:
                    wait(sp, adjT_ready, TURNS * t + CB * (c - RAW + 1))
                else:
                    wait(sp, adjT_ready, TURNS * (t - 1) + (TURNS if c + RAW == CHUNKS - 1 else CB * (c + RAW + 1)))
                for a in range(QUADS):
                    src = adj[bass.ds(row0, rows), col_of(c, a):col_of(c, a) + seg_of(c)]
                    sp.dma_start(raw[c % RAW][SQ * a:SQ * a + SQ, 0:rows // SQ, 0:seg_of(c)],
                                 src.rearrange("(r i) c -> i r c", i=SQ)).then_inc(raw_loaded[c % RAW], 16)

            def load_x(t, par, row0):
                sp.dma_start(x_nat[:, par, :, :],
                             x[bass.ds(row0, ROWS), :].rearrange("(q p) d -> p q d", p=P)
                             ).then_inc(x_loaded[par], 16)

            sp.dma_start(w_raw[:, 0, :], w_item).then_inc(w_loaded, 16)
            sp.dma_start(w_raw[:, 1, :], w_user).then_inc(w_loaded, 16)
            for c in range(CHUNKS):
                for a in range(QUADS):
                    rows = item[col_of(c, a):col_of(c, a) + SEG, :].rearrange("(b j) d -> j b d", j=SQ)
                    sp.dma_start(h[SQ * a:SQ * a + SQ, CB * c:CB * c + CB, :], rows).then_inc(item_loaded[c], 16)
                if c == 0:
                    sp.dma_start(b_item_row[:, :], b_item.rearrange("(o d) -> o d", o=1).to_broadcast([P, D])
                                 ).then_inc(bias_loaded, 16)
                    sp.dma_start(b_user_col[:, :], b_user.rearrange("(d o) -> d o", o=1)).then_inc(bias_loaded, 16)
            sp.wait_ge(item_pad, 1)
            for a in range(QUADS):
                first = col_of(CHUNKS - 1, a) + SEG
                sp.dma_start(h[SQ * a:SQ * a + REST // QUADS, BLOCKS - 1, :],
                             item[first:first + REST // QUADS, :]).then_inc(item_rest_loaded, 16)
            sp.wait_ge(pad_zeroed, 1)
            for c in range(RAW):
                load_chunk(0, 0, ROWS, c)
            load_x(0, 0, 0)
            with sp.Fori(0, PAIRS) as i:
                for par in range(2):
                    t = 2 * i + par
                    for c in range(RAW, CHUNKS):
                        load_chunk(t, ROWS * t, ROWS, c)
                    for c in range(RAW):
                        load_chunk(t + 1, ROWS * t + ROWS, ROWS, c)
                    load_x(t + 1, 1 - par, ROWS * t + ROWS)
            for c in range(RAW, CHUNKS):
                load_chunk(FULL - 1, ROWS * (FULL - 1), ROWS, c)
            for c in range(RAW):
                load_chunk(FULL, NARROW_AT, NARROW, c)
            for q, rows in segments(NARROW):
                sp.dma_start(x_nat[0:rows, FULL % 2, q, :],
                             x[NARROW_AT + P * q:NARROW_AT + P * q + rows, :]).then_inc(x_loaded[FULL % 2], 16)
            for c in range(RAW, CHUNKS):
                load_chunk(FULL, NARROW_AT, NARROW, c)

        @block.gpsimd
        def _(pool):
            nc.gpsimd.memset(ident[:, :], 0.0).then_inc(ident_zero, 1)
            pool.wait_ge(ident_zero, 1)
            nc.gpsimd.affine_select(out=ident[:, :], in_=ident[:, :], compare_op=ALU.not_equal, fill=1.0,
                                    base=0, pattern=[[-1, P]], channel_multiplier=1).then_inc(ident_ready, 1)

        @block.tensor
        def _(pe):
            def blocks(i, par, k0, k1, rows=ROWS, last_out=True):
                t = 2 * i + par
                for k in range(k0, k1):
                    pe.wait_ge(adjT_ready, TURNS * t + k + 1)
                    nc.tensor.matmul(acc[par][:, 0:rows], h[:, k, :], adjT[:, k % SLOTS, 0:rows],
                                     start=(k == 0), stop=(k == BLOCKS - 1)
                                     ).then_inc(adjT_used, TURNS - k if k == BLOCKS - 1 else 1)
                    if k == PE_TURN_OUT and last_out:
                        turn_out(t - 1, ROWS)
                    if k == PE_TURN_X:
                        pe.wait_ge(x_loaded[par], 16 * i + 16 * (1 if rows == ROWS else len(segments(rows))))
                        for q, n in segments(rows):
                            last = nc.tensor.transpose(ps_x[:, P * q:P * q + n], x_nat[0:n, par, q, :],
                                                       ident[0:n, 0:n])
                        last.then_inc(x_turned, 1)
                    if k == PE_ADD_X:
                        pe.wait_ge(xT_ready, t + 1)
                        nc.tensor.matmul(acc[par][:, 0:rows], w_userT[:, :], xT[:, 0:rows],
                                         start=False, stop=False).then_inc(x_done, 1)

            def turn_out(t, rows):
                pe.wait_ge(relu_done, t + 1)
                for q, n in segments(rows):
                    last = nc.tensor.transpose(ps_o[0:n, q, :], act_out[:, P * q:P * q + n], ident[:, :])
                last.then_inc(out_turned, 1)

            pe.wait_ge(ident_ready, 1)
            pe.wait_ge(w_loaded, 32)
            for n in range(2):
                nc.tensor.transpose(ps_t[1][:, n, :], w_raw[:, n, :], ident[:, :]).then_inc(w_turned, 1)

            def turn_items(g):
                pe.wait_ge(item_loaded[chunk_of(min(G * g + G, BLOCKS) - 1)], 16 * QUADS)
                if G * g + G >= BLOCKS:
                    pe.wait_ge(item_rest_loaded, 16 * QUADS)
                wait(pe, itemT_ready, g - 1)
                for j, k in enumerate(range(G * g, min(G * g + G, BLOCKS))):
                    last = nc.tensor.transpose(ps_t[g % 2][:, j, :], h[:, k, :], ident[:, :])
                last.then_inc(item_turned, 1)

            turn_items(0)
            pe.wait_ge(w_ready, 1)
            for g in range(GROUPS):
                if g + 1 < GROUPS:
                    turn_items(g + 1)
                pe.wait_ge(itemT_ready, g + 1)
                wait(pe, h_ready, g - 1)
                for j, k in enumerate(range(G * g, min(G * g + G, BLOCKS))):
                    last = nc.tensor.matmul(ps_h[g % 2][:, j, :], itemT[:, g % 2, j, :], w_itemT[:, :],
                                            start=True, stop=True)
                last.then_inc(h_summed, 1)
            pe.wait_ge(h_ready, GROUPS)

            blocks(0, 0, 0, PE_SKEW, last_out=False)
            with pe.Fori(0, PAIRS) as i:
                blocks(i, 0, PE_SKEW, BLOCKS)
                blocks(i, 1, 0, PE_SKEW)
                blocks(i, 1, PE_SKEW, BLOCKS)
                blocks(i + 1, 0, 0, PE_SKEW)
            blocks(PAIRS, 0, PE_SKEW, BLOCKS)
            blocks(PAIRS, 1, 0, BLOCKS, NARROW)
            turn_out(FULL, NARROW)

        @block.scalar
        def _(act):
            def move_xT(t, rows):
                act.wait_ge(x_turned, t + 1)
                nc.scalar.copy(xT[:, 0:rows], ps_x[:, 0:rows]).then_inc(xT_ready, 1)

            def relu(t, par, rows):
                act.wait_ge(adjT_used, TURNS * t + TURNS)
                act.wait_ge(x_done, t + 1)
                nc.scalar.activation(act_out[:, 0:rows], acc[par][:, 0:rows], ACT.Relu,
                                     bias=b_user_col[:, 0:1]).then_inc(relu_done, 1)

            def root(t):
                act.wait_ge(var_ready, t + 1)
                nc.scalar.activation(std[:, :], mv[:, :, 1], ACT.Sqrt, bias=eps_col[:, 0:1]
                                     ).then_inc(std_ready, 1)

            def store(t, par, row0):
                act.wait_ge(o_ready, t + 1)
                act.dma_start(out[bass.ds(row0, ROWS), :].rearrange("(q p) d -> p q d", p=P),
                              o[:, par, :, :]).then_inc(out_stored[par], 16)

            act.wait_ge(w_turned, 2)
            nc.scalar.copy(w_itemT[:, :], ps_t[1][:, 0, :])
            nc.scalar.copy(w_userT[:, :], ps_t[1][:, 1, :]).then_inc(w_ready, 1)
            for g in range(GROUPS):
                n = min(G, BLOCKS - G * g)
                act.wait_ge(item_turned, g + 1)
                wait(act, h_summed, g - 1)
                nc.scalar.copy(itemT[:, g % 2, 0:n, :], ps_t[g % 2][:, 0:n, :]).then_inc(itemT_ready, 1)
            act.wait_ge(bias_loaded, 32)
            act.wait_ge(consts_set, 1)
            move_xT(0, ROWS)
            with act.Fori(0, PAIRS) as i:
                for par in range(2):
                    t = 2 * i + par
                    relu(t, par, ROWS)
                    root(t)
                    store(t, par, ROWS * t)
                    move_xT(t + 1, ROWS)
                    act.wait_ge(out_stored[par], 16 * i + 16)
            relu(FULL - 1, 0, ROWS)
            root(FULL - 1)
            store(FULL - 1, 0, ROWS * (FULL - 1))
            move_xT(FULL, NARROW)
            relu(FULL, 1, NARROW)
            root(FULL)
            act.wait_ge(o_ready, FULL + 1)
            for q, n in segments(NARROW):
                lo = DOUBLE if q == 0 else 0
                act.dma_start(out[NARROW_AT + P * q + lo:NARROW_AT + P * q + n, :], o[lo:n, 1, q, :]
                              ).then_inc(out_stored[1], 16)
            act.wait_ge(out_stored[0], 16 * (PAIRS + 1))
            act.wait_ge(out_stored[1], 16 * PAIRS + 16 * len(segments(NARROW)))

        @block.vector
        def _(dve):
            def blocks(i, par, k0, k1, rows=ROWS, last_out=True):
                t = 2 * i + par
                for k in range(k0, k1):
                    c = chunk_of(k)
                    if k == CB * c:
                        fills = CHUNKS // RAW * t + c // RAW + 1
                        dve.wait_ge(raw_loaded[c % RAW], 16 * QUADS * fills)
                    wait(dve, adjT_used, TURNS * t + k - SLOTS + 1)
                    if k == V_VAR and last_out:
                        dve.wait_ge(stats_ready, t)
                    b = k - CB * c
                    turned = nc.vector.transpose(
                        adjT[:, k % SLOTS, 0:rows].rearrange("p (r i) -> p r i", i=SQ),
                        raw[c % RAW][:, 0:rows // SQ, SQ * b:SQ * b + SQ])
                    turned.then_inc(adjT_ready, TURNS - k if k == BLOCKS - 1 else 1)
                    if last_out:
                        finish(k, i if par == 1 else i - 1, 1 - par, ROWS)

            def finish(k, i, par, rows):
                t = 2 * i + par
                if k == V_RESIDUAL:
                    dve.wait_ge(out_turned, t + 1)
                    for q, n in segments(rows):
                        last = nc.vector.tensor_tensor(y[0:n, q, :], ps_o[0:n, q, :], x_nat[0:n, par, q, :], ALU.add)
                    last.then_inc(y_ready, 1)
                if k == V_STATS:
                    dve.wait_ge(y_ready, t + 1)
                    for q, n in segments(rows):
                        last = nc.vector.bn_stats(stats[0:n, q, :], y[0:n, q, :])
                    last.then_inc(stats_ready, 1)
                if k == V_VAR:
                    if isinstance(t, int):
                        dve.wait_ge(stats_ready, t + 1)
                    for q, n in segments(rows):
                        last = nc.vector.bn_aggr(mv[0:n, q, :], stats[0:n, q, :])
                    last.then_inc(var_ready, 1)
                if k == V_RSTD:
                    dve.wait_ge(std_ready, t + 1)
                    nc.vector.reciprocal(rstd[:, :], std[:, :]).then_inc(rstd_ready, 1)
                if k == V_NORM:
                    dve.wait_ge(rstd_ready, t + 1)
                    for q, n in segments(rows):
                        last = nc.vector.tensor_scalar(o[0:n, par, q, :], y[0:n, q, :], mv[0:n, q, 0:1],
                                                       rstd[0:n, q:q + 1], ALU.subtract, ALU.mult)
                    last.then_inc(o_ready, 1)

            nc.vector.memset(h[:, BLOCKS - 1, :], 0.0).then_inc(item_pad, 1)
            nc.vector.memset(raw[(CHUNKS - 1) % RAW][:, :, SEG:PAD_SEG], 0.0).then_inc(pad_zeroed, 1)
            nc.vector.memset(eps_col[:, :], EPS).then_inc(consts_set, 1)
            dve.wait_ge(bias_loaded, 32)
            for g in range(GROUPS):
                n = min(G, BLOCKS - G * g)
                dve.wait_ge(h_summed, g + 1)
                nc.vector.tensor_tensor(h[:, G * g:G * g + n, :], ps_h[g % 2][:, 0:n, :],
                                        b_item_row[:, :].rearrange("p (o d) -> p o d", o=1).to_broadcast([P, n, D]),
                                        ALU.add).then_inc(h_ready, 1)

            blocks(0, 0, 0, V_SKEW, last_out=False)
            with dve.Fori(0, PAIRS) as i:
                blocks(i, 0, V_SKEW, BLOCKS)
                blocks(i, 1, 0, V_SKEW)
                blocks(i, 1, V_SKEW, BLOCKS)
                blocks(i + 1, 0, 0, V_SKEW)
            blocks(PAIRS, 0, V_SKEW, BLOCKS)
            blocks(PAIRS, 1, 0, BLOCKS, NARROW)
            for k in (V_RESIDUAL, V_STATS, V_VAR, V_RSTD, V_NORM):
                finish(k, PAIRS, 1, NARROW)


_INS = ["x", "adj", "L0_gnn_item_feat", "L0_gnn_W_item", "L0_gnn_b_item", "L0_gnn_W_user", "L0_gnn_b_user"]


def kernel(**inputs):
    import numpy as _np
    import concourse.bacc as _bacc
    from concourse import mybir as _mybir
    from concourse.bass_utils import run_bass_kernel_spmd as _run

    nc = _bacc.Bacc("TRN2", target_bir_lowering=False, num_devices=1)
    arrays, args = {}, []
    for name in _INS:
        a = _np.ascontiguousarray(inputs[name])
        arrays[f"in_{name}_dram"] = a
        args.append(nc.dram_tensor(f"in_{name}_dram", a.shape, _mybir.dt.from_np(a.dtype), kind="ExternalInput").ap())
    args.append(nc.dram_tensor("out_0_dram", (N, D), _mybir.dt.float32, kind="ExternalOutput").ap())
    build(nc, *args)
    return _run(nc, [arrays], core_ids=[0]).results[0]["out_0_dram"]
```

```python
from contextlib import ExitStack

import concourse.bass as bass
from concourse import mybir

FP32 = mybir.dt.float32
FP32R = mybir.dt.float32r
ALU = mybir.AluOpType
ACT = mybir.ActivationFunctionType

P = 128
SQ = 32
QUADS = P // SQ
N = 10000
D = 128
EPS = 1e-5

CHUNK_BLOCKS = [14, 14, 12, 14, 12, 12]
CHUNKS = len(CHUNK_BLOCKS)
CHUNK_AT = [sum(CHUNK_BLOCKS[:c]) for c in range(CHUNKS + 1)]
REST = N - CHUNK_AT[CHUNKS] * P
BLOCKS = CHUNK_AT[CHUNKS] + 1
RAW = 3
RAW_COLS = [448, 448, 416]
assert SQ * max(CHUNK_BLOCKS) == RAW_COLS[0]
assert SQ * (CHUNK_BLOCKS[CHUNKS - 1] + 1) == RAW_COLS[RAW - 1] and CHUNK_BLOCKS[2] == CHUNK_BLOCKS[5]

U = 2
UNITS = -(-BLOCKS // U)
WHOLE, SPLIT_G, SPLIT_V = range(3)
PATTERN = "GGWGWVGGWGGWGGWGGWVGGWGWGWGGWGGWGWVGGVG"
KIND = [{"G": SPLIT_G, "V": SPLIT_V, "W": WHOLE}[kind] for kind in PATTERN for _ in range(U)] + [WHOLE]
assert len(KIND) == BLOCKS
IN_SBUF = [k for k in range(BLOCKS) if KIND[k] != SPLIT_V]
IN_PSUM = [k for k in range(BLOCKS) if KIND[k] == SPLIT_V]
SPLIT = [k for k in range(BLOCKS) if KIND[k] != WHOLE]
BY_G = [k for k in range(BLOCKS) if KIND[k] == SPLIT_G]
PLAIN = [k for k in range(BLOCKS) if KIND[k] == WHOLE]
T_SLOTS = 8
V_SLOTS = 4
S_SLOTS = 6
LAG = 3
FIRST = min(range(BLOCKS), key=lambda k: k + (LAG if k in SPLIT else -0.5))
LAST = max(range(BLOCKS), key=lambda k: k + (LAG if k in SPLIT else -0.5))

ROWS = 512
FULL = N // ROWS
NARROW = -(-(N - FULL * ROWS) // SQ) * SQ
NARROW_AT = N - NARROW
DOUBLE = FULL * ROWS - NARROW_AT
PAIRS = (FULL - 1) // 2

A_RELU, PE_TURN_OUT, V_RESIDUAL, V_STATS, V_VAR, A_ROOT, V_RSTD, V_NORM, A_STORE, A_STORED = \
    10, 11, 22, 23, 26, 30, 32, 34, 38, 42
PE_TURN_X, A_MOVE_X, PE_ADD_X = 50, 60, 66
SKEW = 44


def chunk_of(k):
    return next(c for c in range(CHUNKS) if k < CHUNK_AT[c + 1] or c == CHUNKS - 1)


def chunk_end(c):
    return BLOCKS if c == CHUNKS - 1 else CHUNK_AT[c + 1]


def seg_of(c):
    return SQ * CHUNK_BLOCKS[c] + (REST // QUADS if c == CHUNKS - 1 else 0)


def col_of(c, a):
    return CHUNK_AT[c] * P + a * seg_of(c)


def slot(among, slots, k):
    return among.index(k) % slots


def done(t, among, k):
    return len(among) * t + among.index(k) + 1


def before(t, among, slots, k):
    n = among.index(k) - slots
    if n >= 0:
        return t, among[n]
    return t - 1, [b for b in among if slot(among, slots, b) == slot(among, slots, k)][-1]


def segments(rows):
    return [(q, min(P, rows - q * P)) for q in range(-(-rows // P))]


def wait(eng, semaphore, count):
    if not isinstance(count, int) or count > 0:
        eng.wait_ge(semaphore, count)


def build(nc, x, adj, item, w_item, b_item, w_user, b_user, out):
    ctx = ExitStack()
    with ctx:
        def sb(name, shape, dtype=FP32):
            return ctx.enter_context(nc.sbuf_tensor(name, shape, dtype))

        def ps(name, shape):
            return ctx.enter_context(nc.psum_tensor(name, shape, FP32))

        def sem(name):
            return ctx.enter_context(nc.semaphore(name))

        h = sb("h", [P, len(PLAIN), D])
        h_hi = sb("h_hi", [P, len(SPLIT), D], FP32R)
        h_lo = sb("h_lo", [P, len(SPLIT), D], FP32R)
        raw = [sb(f"raw{i}", [P, ROWS // SQ, RAW_COLS[i]]) for i in range(RAW)]
        adjT = sb("adjT", [P, T_SLOTS, ROWS])
        adj_hi = sb("adj_hi", [P, S_SLOTS, ROWS], FP32R)
        adj_lo = sb("adj_lo", [P, S_SLOTS, ROWS], FP32R)
        ident = sb("ident", [P, P])
        w_raw = sb("w_raw", [P, 2, D])
        w_itemT = sb("w_itemT", [P, D])
        w_userT = sb("w_userT", [P, D])
        b_item_row = sb("b_item_row", [P, D])
        b_user_col = sb("b_user_col", [P, 1])
        eps_col = sb("eps_col", [P, 1])
        item_rest = sb("item_rest", [P, D])
        x_nat = sb("x_nat", [P, 2, ROWS // P, D])
        xT = sb("xT", [P, ROWS])
        act_out = sb("act_out", [P, ROWS])
        y = sb("y", [P, ROWS // P, D])
        stats = sb("stats", [P, ROWS // P, 6])
        mv = sb("mv", [P, ROWS // P, 2])
        std = sb("std", [P, ROWS // P])
        rstd = sb("rstd", [P, ROWS // P])
        o = sb("o", [P, 2, ROWS // P, D])
        stage = [raw[RAW - 1][:, :, :].rearrange("p r c -> p (r c)").rearrange("p (b d) -> p b d", d=D),
                 adjT[:, :, :].rearrange("p s (b d) -> p (s b) d", d=D)]
        STAGE = ROWS // SQ * RAW_COLS[RAW - 1] // D
        assert BLOCKS - 1 - STAGE <= T_SLOTS * ROWS // D
        STAGED_U = -(-STAGE // U)
        itemT = act_out[:, :].rearrange("p (s u d) -> p s u d", s=2, u=U)
        H_SLOTS = 2 * ROWS // D // U
        h_sum = o[:, :, :, :].rearrange("p g (s u) d -> p (g s) u d", u=U)

        acc = [ps(f"acc{i}", [P, ROWS]) for i in range(2)]
        adjT_ps = ps("adjT_ps", [P, V_SLOTS, ROWS])
        ps_x = ps("ps_x", [P, ROWS])
        ps_o = ps("ps_o", [P, ROWS // P, D])
        ps_t = [adjT_ps[:, i, 0:U * D].rearrange("p (u d) -> p u d", u=U) for i in range(2)]
        ps_h = [adjT_ps[:, 2 + i, 0:U * D].rearrange("p (u d) -> p u d", u=U) for i in range(2)]

        ident_zero = sem("ident_zero")
        ident_ready = sem("ident_ready")
        w_loaded = sem("w_loaded")
        bias_loaded = sem("bias_loaded")
        rest_zeroed = sem("rest_zeroed")
        item_loaded = [sem(f"item_loaded{c}") for c in range(CHUNKS)]
        item_rest_loaded = sem("item_rest_loaded")
        w_turned = sem("w_turned")
        w_ready = sem("w_ready")
        item_turned = sem("item_turned")
        itemT_ready = sem("itemT_ready")
        h_product = sem("h_product")
        h_sum_ready = sem("h_sum_ready")
        h_hi_ready = sem("h_hi_ready")
        h_lo_ready = sem("h_lo_ready")
        consts_set = sem("consts_set")
        pad_zeroed = sem("pad_zeroed")
        raw_loaded = [sem(f"raw_loaded{i}") for i in range(RAW)]
        turned = sem("turned")
        hi_ready = sem("hi_ready")
        lo_ready_g = sem("lo_ready_g")
        lo_ready_v = sem("lo_ready_v")
        whole_used = sem("whole_used")
        split_used = sem("split_used")
        x_loaded = [sem(f"x_loaded{i}") for i in range(2)]
        x_turned = sem("x_turned")
        xT_ready = sem("xT_ready")
        x_done = sem("x_done")
        relu_done = sem("relu_done")
        out_turned = sem("out_turned")
        y_ready = sem("y_ready")
        stats_ready = sem("stats_ready")
        var_ready = sem("var_ready")
        std_ready = sem("std_ready")
        rstd_ready = sem("rstd_ready")
        o_ready = sem("o_ready")
        out_stored = [sem(f"out_stored{i}") for i in range(2)]

        def pieces(c):
            lo, hi = CHUNK_AT[c], CHUNK_AT[c + 1]
            mid = min(max(STAGE, lo), hi)
            return [(s, b - s * STAGE, b - lo, n) for s, b, n in ((0, lo, mid - lo), (1, mid, hi - mid)) if n]

        def loads_of(c):
            return 16 * QUADS * len(pieces(c))

        block = ctx.enter_context(nc.Block())

        @block.sync
        def _(sp):
            def load_chunk(t, row0, rows, c):
                if c >= RAW:
                    wait(sp, turned, BLOCKS * t + chunk_end(c - RAW))
                else:
                    wait(sp, turned, BLOCKS * (t - 1) + chunk_end(c + RAW))
                for a in range(QUADS):
                    src = adj[bass.ds(row0, rows), col_of(c, a):col_of(c, a) + seg_of(c)]
                    sp.dma_start(raw[c % RAW][SQ * a:SQ * a + SQ, 0:rows // SQ, 0:seg_of(c)],
                                 src.rearrange("(r i) c -> i r c", i=SQ)).then_inc(raw_loaded[c % RAW], 16)

            def load_x(par, row0):
                sp.dma_start(x_nat[:, par, :, :],
                             x[bass.ds(row0, ROWS), :].rearrange("(q p) d -> p q d", p=P)
                             ).then_inc(x_loaded[par], 16)

            def load_items(c):
                for s, at, b0, n in pieces(c):
                    for a in range(QUADS):
                        first = col_of(c, a) + SQ * b0
                        sp.dma_start(stage[s][SQ * a:SQ * a + SQ, at:at + n, :],
                                      item[first:first + SQ * n, :].rearrange("(b j) d -> j b d", j=SQ)
                                      ).then_inc(item_loaded[c], 16)

            sp.dma_start(w_raw[:, 0, :], w_item).then_inc(w_loaded, 16)
            sp.dma_start(w_raw[:, 1, :], w_user).then_inc(w_loaded, 16)
            load_items(0)
            sp.dma_start(b_item_row[:, :], b_item.rearrange("(o d) -> o d", o=1).to_broadcast([P, D])
                         ).then_inc(bias_loaded, 16)
            sp.dma_start(b_user_col[:, :], b_user.rearrange("(d o) -> d o", o=1)).then_inc(bias_loaded, 16)
            for c in range(1, CHUNKS):
                load_items(c)
            sp.wait_ge(rest_zeroed, 1)
            for a in range(QUADS):
                first = col_of(CHUNKS - 1, a) + seg_of(CHUNKS - 1) - REST // QUADS
                sp.dma_start(item_rest[SQ * a:SQ * a + REST // QUADS, :],
                              item[first:first + REST // QUADS, :]).then_inc(item_rest_loaded, 16)
            for c in range(RAW):
                if c == RAW - 1:
                    sp.wait_ge(pad_zeroed, 1)
                load_chunk(0, 0, ROWS, c)
            load_x(0, 0)
            with sp.Fori(0, PAIRS) as i:
                for par in range(2):
                    t = 2 * i + par
                    for c in range(RAW, CHUNKS):
                        load_chunk(t, ROWS * t, ROWS, c)
                    for c in range(RAW):
                        load_chunk(t + 1, ROWS * t + ROWS, ROWS, c)
                    load_x(1 - par, ROWS * t + ROWS)
            for c in range(RAW, CHUNKS):
                load_chunk(FULL - 1, ROWS * (FULL - 1), ROWS, c)
            for c in range(RAW):
                load_chunk(FULL, NARROW_AT, NARROW, c)
            for q, rows in segments(NARROW):
                sp.dma_start(x_nat[0:rows, FULL % 2, q, :],
                             x[NARROW_AT + P * q:NARROW_AT + P * q + rows, :]).then_inc(x_loaded[FULL % 2], 16)
            for c in range(RAW, CHUNKS):
                load_chunk(FULL, NARROW_AT, NARROW, c)

        @block.gpsimd
        def _(pool):
            nc.gpsimd.memset(ident[:, :], 0.0).then_inc(ident_zero, 1)
            pool.wait_ge(ident_zero, 1)
            nc.gpsimd.affine_select(out=ident[:, :], in_=ident[:, :], compare_op=ALU.not_equal, fill=1.0,
                                    base=0, pattern=[[-1, P]], channel_multiplier=1).then_inc(ident_ready, 1)

            def blocks(t, k0, k1, rows=ROWS):
                for k in range(k0, k1):
                    if KIND[k] == SPLIT_G:
                        pool.wait_ge(hi_ready, done(t, SPLIT, k))
                        s = slot(SPLIT, S_SLOTS, k)
                        nc.gpsimd.tensor_tensor(adj_lo[:, s, 0:rows], adjT[:, slot(IN_SBUF, T_SLOTS, k), 0:rows],
                                                adj_hi[:, s, 0:rows].bitcast(FP32), ALU.subtract
                                                ).then_inc(lo_ready_g, 1)

            for n in range(len(SPLIT) // U):
                pool.wait_ge(h_hi_ready, n + 1)
                nc.gpsimd.tensor_tensor(h_lo[:, U * n:U * n + U, :], h_sum[:, n % H_SLOTS, :, :],
                                        h_hi[:, U * n:U * n + U, :].bitcast(FP32), ALU.subtract
                                        ).then_inc(h_lo_ready, 1)

            blocks(0, 0, SKEW)
            with pool.Fori(0, FULL - 1) as t:
                blocks(t, SKEW, BLOCKS)
                blocks(t + 1, 0, SKEW)
            blocks(FULL - 1, SKEW, BLOCKS)
            blocks(FULL, 0, BLOCKS, NARROW)

        @block.tensor
        def _(pe):
            def blocks(i, par, k0, k1, rows=ROWS, last_out=True):
                t = 2 * i + par
                for k in range(k0, k1):
                    if k == PE_TURN_OUT and last_out:
                        turn_out(t - 1, ROWS)
                    if k == PE_TURN_X:
                        pe.wait_ge(x_loaded[par], 16 * i + 16 * (1 if rows == ROWS else len(segments(rows))))
                        for q, n in segments(rows):
                            last = nc.tensor.transpose(ps_x[:, P * q:P * q + n], x_nat[0:n, par, q, :],
                                                       ident[0:n, 0:n])
                        last.then_inc(x_turned, 1)
                    if k == PE_ADD_X:
                        pe.wait_ge(xT_ready, t + 1)
                        nc.tensor.matmul(acc[par][:, 0:rows], w_userT[:, :], xT[:, 0:rows],
                                         start=False, stop=False).then_inc(x_done, 1)
                    if KIND[k] == WHOLE:
                        pe.wait_ge(turned, BLOCKS * t + k + 1)
                        nc.tensor.matmul(acc[par][:, 0:rows], h[:, PLAIN.index(k), :],
                                         adjT[:, slot(IN_SBUF, T_SLOTS, k), 0:rows],
                                         start=(k == FIRST), stop=(k == LAST)).then_inc(whole_used, 1)
                    if k >= LAG:
                        split_block(t, par, k - LAG, rows)
                    elif last_out:
                        split_block(t - 1, 1 - par, k - LAG + BLOCKS, ROWS)

            def split_block(t, par, k, rows):
                if KIND[k] == WHOLE:
                    return
                if KIND[k] == SPLIT_G:
                    pe.wait_ge(lo_ready_g, done(t, BY_G, k))
                else:
                    pe.wait_ge(lo_ready_v, done(t, IN_PSUM, k))
                n, s = SPLIT.index(k), slot(SPLIT, S_SLOTS, k)
                for part, (a, w) in enumerate(((adj_hi, h_hi), (adj_hi, h_lo), (adj_lo, h_hi))):
                    last = nc.tensor.matmul(acc[par][:, 0:rows], w[:, n, :], a[:, s, 0:rows],
                                            start=(k == FIRST and part == 0), stop=(k == LAST and part == 2))
                last.then_inc(split_used, 1)

            def turn_out(t, rows):
                pe.wait_ge(relu_done, t + 1)
                for q, n in segments(rows):
                    last = nc.tensor.transpose(ps_o[0:n, q, :], act_out[:, P * q:P * q + n], ident[:, :])
                last.then_inc(out_turned, 1)

            pe.wait_ge(ident_ready, 1)
            pe.wait_ge(w_loaded, 32)
            for n in range(2):
                last = nc.tensor.transpose(ps_t[1][:, n, :], w_raw[:, n, :], ident[:, :])
            last.then_inc(w_turned, 1)

            def turn_items(u):
                c = chunk_of(U * u)
                pe.wait_ge(item_loaded[c], loads_of(c))
                if u == 1:
                    pe.wait_ge(w_ready, 1)
                wait(pe, itemT_ready, u - 1)
                for j, k in enumerate(range(U * u, min(U * u + U, BLOCKS))):
                    if k == BLOCKS - 1:
                        pe.wait_ge(item_rest_loaded, 16 * QUADS)
                        src = item_rest[:, :]
                    else:
                        src = stage[k // STAGE][:, k % STAGE, :]
                    last = nc.tensor.transpose(ps_t[u % 2][:, j, :], src, ident[:, :])
                last.then_inc(item_turned, 1)

            turn_items(0)
            turn_items(1)
            for u in range(UNITS):
                pe.wait_ge(itemT_ready, u + 1)
                wait(pe, h_sum_ready, u - 1)
                for j, k in enumerate(range(U * u, min(U * u + U, BLOCKS))):
                    last = nc.tensor.matmul(ps_h[u % 2][:, j, :], itemT[:, u % 2, j, :], w_itemT[:, :],
                                            start=True, stop=True)
                last.then_inc(h_product, 1)
                if u + 2 < UNITS:
                    turn_items(u + 2)
            pe.wait_ge(h_lo_ready, len(SPLIT) // U)
            pe.wait_ge(h_sum_ready, UNITS)

            blocks(0, 0, 0, SKEW, last_out=False)
            with pe.Fori(0, PAIRS) as i:
                blocks(i, 0, SKEW, BLOCKS)
                blocks(i, 1, 0, SKEW)
                blocks(i, 1, SKEW, BLOCKS)
                blocks(i + 1, 0, 0, SKEW)
            blocks(PAIRS, 0, SKEW, BLOCKS)
            blocks(PAIRS, 1, 0, BLOCKS, NARROW)
            for k in range(BLOCKS - LAG, BLOCKS):
                split_block(FULL, 1, k, NARROW)
            turn_out(FULL, NARROW)

        @block.scalar
        def _(act):
            def blocks(i, par, k0, k1, rows=ROWS, last_out=True):
                t = 2 * i + par
                for k in range(k0, k1):
                    if last_out:
                        finish(k, i if par == 1 else i - 1, 1 - par)
                    if k == A_MOVE_X:
                        act.wait_ge(x_turned, t + 1)
                        nc.scalar.copy(xT[:, 0:rows], ps_x[:, 0:rows]).then_inc(xT_ready, 1)
                    if KIND[k] == WHOLE:
                        continue
                    act.wait_ge(turned, BLOCKS * t + k + 1)
                    bt, bk = before(t, SPLIT, S_SLOTS, k)
                    wait(act, split_used, done(bt, SPLIT, bk))
                    if KIND[k] == SPLIT_G:
                        src = adjT[:, slot(IN_SBUF, T_SLOTS, k), 0:rows]
                    else:
                        src = adjT_ps[:, slot(IN_PSUM, V_SLOTS, k), 0:rows]
                    nc.scalar.copy(adj_hi[:, slot(SPLIT, S_SLOTS, k), 0:rows], src).then_inc(hi_ready, 1)

            def finish(k, i, par):
                t = 2 * i + par
                if k == A_RELU:
                    relu(t, par, ROWS)
                if k == A_ROOT:
                    root(t)
                if k == A_STORE:
                    act.wait_ge(o_ready, t + 1)
                    act.dma_start(out[bass.ds(ROWS * t, ROWS), :].rearrange("(q p) d -> p q d", p=P),
                                  o[:, par, :, :]).then_inc(out_stored[par], 16)
                if k == A_STORED:
                    act.wait_ge(out_stored[par], 16 * i + 16)

            def relu(t, par, rows):
                act.wait_ge(split_used, len(SPLIT) * (t + 1))
                act.wait_ge(whole_used, len(PLAIN) * (t + 1))
                act.wait_ge(x_done, t + 1)
                nc.scalar.activation(act_out[:, 0:rows], acc[par][:, 0:rows], ACT.Relu,
                                     bias=b_user_col[:, 0:1]).then_inc(relu_done, 1)

            def root(t):
                act.wait_ge(var_ready, t + 1)
                nc.scalar.activation(std[:, :], mv[:, :, 1], ACT.Sqrt, bias=eps_col[:, 0:1]
                                     ).then_inc(std_ready, 1)

            act.wait_ge(w_turned, 1)
            nc.scalar.copy(w_itemT[:, :], ps_t[1][:, 0, :])
            nc.scalar.copy(w_userT[:, :], ps_t[1][:, 1, :]).then_inc(w_ready, 1)

            for u in range(UNITS):
                if U * u in SPLIT:
                    n = SPLIT.index(U * u)
                    act.wait_ge(h_sum_ready, u + 1)
                    nc.scalar.copy(h_hi[:, n:n + U, :], h_sum[:, n // U % H_SLOTS, :, :]).then_inc(h_hi_ready, 1)
            act.wait_ge(bias_loaded, 32)
            act.wait_ge(consts_set, 1)

            blocks(0, 0, 0, SKEW, last_out=False)
            with act.Fori(0, PAIRS) as i:
                blocks(i, 0, SKEW, BLOCKS)
                blocks(i, 1, 0, SKEW)
                blocks(i, 1, SKEW, BLOCKS)
                blocks(i + 1, 0, 0, SKEW)
            blocks(PAIRS, 0, SKEW, BLOCKS)
            blocks(PAIRS, 1, 0, BLOCKS, NARROW)
            relu(FULL, 1, NARROW)
            root(FULL)
            act.wait_ge(o_ready, FULL + 1)
            for q, n in segments(NARROW):
                lo = DOUBLE if q == 0 else 0
                act.dma_start(out[NARROW_AT + P * q + lo:NARROW_AT + P * q + n, :], o[lo:n, 1, q, :]
                              ).then_inc(out_stored[1], 16)
            act.wait_ge(out_stored[0], 16 * (PAIRS + 1))
            act.wait_ge(out_stored[1], 16 * PAIRS + 16 * len(segments(NARROW)))

        @block.vector
        def _(dve):
            def blocks(i, par, k0, k1, rows=ROWS, last_out=True):
                t = 2 * i + par
                for k in range(k0, k1):
                    c = chunk_of(k)
                    if last_out:
                        finish(k, i if par == 1 else i - 1, 1 - par, ROWS)
                    if k == CHUNK_AT[c]:
                        fills = CHUNKS // RAW * t + c // RAW + 1
                        dve.wait_ge(raw_loaded[c % RAW], 16 * QUADS * fills)
                    if k == V_VAR and last_out:
                        dve.wait_ge(stats_ready, t)
                    if k % U == 0:
                        turn(t, k, min(U, BLOCKS - k), rows)
                    if k == V_VAR and last_out:
                        variance(ROWS)
                    if k >= 2 and KIND[k - 2] == SPLIT_V:
                        low(t, k - 2, rows)

            def turn(t, k, n, rows):
                for b in range(k, k + n):
                    if KIND[b] == SPLIT_V:
                        bt, bk = before(t, IN_PSUM, V_SLOTS, b)
                        wait(dve, lo_ready_v, done(bt, IN_PSUM, bk))
                    elif KIND[before(t, IN_SBUF, T_SLOTS, b)[1]] == SPLIT_G:
                        bt, bk = before(t, IN_SBUF, T_SLOTS, b)
                        wait(dve, lo_ready_g, done(bt, BY_G, bk))
                    else:
                        bt, bk = before(t, IN_SBUF, T_SLOTS, b)
                        wait(dve, whole_used, done(bt, PLAIN, bk))
                if KIND[k] == SPLIT_V:
                    s = slot(IN_PSUM, V_SLOTS, k)
                    dst = adjT_ps[:, s:s + n, 0:rows]
                else:
                    s = slot(IN_SBUF, T_SLOTS, k)
                    dst = adjT[:, s:s + n, 0:rows]
                c = chunk_of(k)
                col = SQ * (k - CHUNK_AT[c])
                src = raw[c % RAW][:, 0:rows // SQ, col:col + SQ * n].rearrange("p r (b j) -> p b r j", j=SQ)
                nc.vector.transpose(dst.rearrange("p b (r i) -> p b r i", i=SQ), src).then_inc(turned, n)

            def low(t, k, rows):
                dve.wait_ge(hi_ready, done(t, SPLIT, k))
                s, v = slot(SPLIT, S_SLOTS, k), slot(IN_PSUM, V_SLOTS, k)
                nc.vector.tensor_tensor(adj_lo[:, s, 0:rows], adjT_ps[:, v, 0:rows],
                                        adj_hi[:, s, 0:rows].bitcast(FP32), ALU.subtract).then_inc(lo_ready_v, 1)

            def variance(rows):
                for q, n in segments(rows):
                    last = nc.vector.bn_aggr(mv[0:n, q, :], stats[0:n, q, :])
                last.then_inc(var_ready, 1)

            def finish(k, i, par, rows):
                t = 2 * i + par
                if k == V_RESIDUAL:
                    dve.wait_ge(out_turned, t + 1)
                    for q, n in segments(rows):
                        last = nc.vector.tensor_tensor(y[0:n, q, :], ps_o[0:n, q, :], x_nat[0:n, par, q, :], ALU.add)
                    last.then_inc(y_ready, 1)
                if k == V_STATS:
                    dve.wait_ge(y_ready, t + 1)
                    for q, n in segments(rows):
                        last = nc.vector.bn_stats(stats[0:n, q, :], y[0:n, q, :])
                    last.then_inc(stats_ready, 1)
                if k == V_RSTD:
                    dve.wait_ge(std_ready, t + 1)
                    nc.vector.reciprocal(rstd[:, :], std[:, :]).then_inc(rstd_ready, 1)
                if k == V_NORM:
                    dve.wait_ge(rstd_ready, t + 1)
                    for q, n in segments(rows):
                        last = nc.vector.tensor_scalar(o[0:n, par, q, :], y[0:n, q, :], mv[0:n, q, 0:1],
                                                       rstd[0:n, q:q + 1], ALU.subtract, ALU.mult)
                    last.then_inc(o_ready, 1)

            nc.vector.memset(item_rest[:, :], 0.0).then_inc(rest_zeroed, 1)
            nc.vector.memset(eps_col[:, :], EPS).then_inc(consts_set, 1)

            def move_items(u):
                n = min(U, BLOCKS - U * u)
                dve.wait_ge(item_turned, u + 1)
                wait(dve, h_product, u - 1)
                nc.vector.tensor_copy(itemT[:, u % 2, 0:n, :], ps_t[u % 2][:, 0:n, :]).then_inc(itemT_ready, 1)

            move_items(0)
            move_items(1)
            dve.wait_ge(bias_loaded, 32)
            for u in range(UNITS):
                n = min(U, BLOCKS - U * u)
                dve.wait_ge(h_product, u + 1)
                if U * u in SPLIT:
                    m = SPLIT.index(U * u) // U
                    wait(dve, h_lo_ready, m - H_SLOTS + 1)
                    dst = h_sum[:, m % H_SLOTS, :, :]
                else:
                    dst = h[:, PLAIN.index(U * u):PLAIN.index(U * u) + n, :]
                nc.vector.tensor_tensor(dst, ps_h[u % 2][:, 0:n, :],
                                        b_item_row[:, :].rearrange("p (o d) -> p o d", o=1).to_broadcast([P, n, D]),
                                        ALU.add).then_inc(h_sum_ready, 1)
                if u + 2 < UNITS:
                    move_items(u + 2)
                if u + 3 == STAGED_U:
                    nc.vector.memset(raw[RAW - 1][:, :, SQ * CHUNK_BLOCKS[RAW - 1]:], 0.0).then_inc(pad_zeroed, 1)

            blocks(0, 0, 0, SKEW, last_out=False)
            with dve.Fori(0, PAIRS) as i:
                blocks(i, 0, SKEW, BLOCKS)
                blocks(i, 1, 0, SKEW)
                blocks(i, 1, SKEW, BLOCKS)
                blocks(i + 1, 0, 0, SKEW)
            blocks(PAIRS, 0, SKEW, BLOCKS)
            blocks(PAIRS, 1, 0, BLOCKS, NARROW)
            finish(V_RESIDUAL, PAIRS, 1, NARROW)
            finish(V_STATS, PAIRS, 1, NARROW)
            dve.wait_ge(stats_ready, FULL + 1)
            variance(NARROW)
            finish(V_RSTD, PAIRS, 1, NARROW)
            finish(V_NORM, PAIRS, 1, NARROW)


_INS = ["x", "adj", "L0_gnn_item_feat", "L0_gnn_W_item", "L0_gnn_b_item", "L0_gnn_W_user", "L0_gnn_b_user"]


def kernel(**inputs):
    import numpy as _np
    import concourse.bacc as _bacc
    from concourse import mybir as _mybir
    from concourse.bass_utils import run_bass_kernel_spmd as _run

    nc = _bacc.Bacc("TRN2", target_bir_lowering=False, num_devices=1)
    arrays, args = {}, []
    for name in _INS:
        a = _np.ascontiguousarray(inputs[name])
        arrays[f"in_{name}_dram"] = a
        args.append(nc.dram_tensor(f"in_{name}_dram", a.shape, _mybir.dt.from_np(a.dtype), kind="ExternalInput").ap())
    args.append(nc.dram_tensor("out_0_dram", (N, D), _mybir.dt.float32, kind="ExternalOutput").ap())
    build(nc, *args)
    return _run(nc, [arrays], core_ids=[0]).results[0]["out_0_dram"]
```

```python
from contextlib import ExitStack

import concourse.bass as bass
from concourse import mybir

FP32 = mybir.dt.float32
FP32R = mybir.dt.float32r
ALU = mybir.AluOpType
ACT = mybir.ActivationFunctionType

P = 128
SQ = 32
QUADS = P // SQ
N = 10000
D = 128
EPS = 1e-5

CHUNK_BLOCKS = [14, 14, 12, 14, 12, 12]
CHUNKS = len(CHUNK_BLOCKS)
CHUNK_AT = [sum(CHUNK_BLOCKS[:c]) for c in range(CHUNKS + 1)]
REST = N - CHUNK_AT[CHUNKS] * P
BLOCKS = CHUNK_AT[CHUNKS] + 1
REST_SEG = REST // QUADS
REST_COPIES = 5
RAW = 3
RAW_COLS = [448, 448, 416]
assert SQ * max(CHUNK_BLOCKS) == RAW_COLS[0]
assert SQ * (CHUNK_BLOCKS[CHUNKS - 1] + 1) == RAW_COLS[RAW - 1] and CHUNK_BLOCKS[2] == CHUNK_BLOCKS[5]

U = 2
UNITS = -(-BLOCKS // U)
WHOLE, SPLIT_G, SPLIT_V, REST_BLOCK = range(4)
PATTERN = "GVGWGWGWGGGWGVWGGWGWGWGGWVGGGWVGGGWWVGG"
KIND = [{"G": SPLIT_G, "V": SPLIT_V, "W": WHOLE}[kind] for kind in PATTERN for _ in range(U)] + [REST_BLOCK]
assert len(KIND) == BLOCKS
IN_SBUF = [k for k in range(BLOCKS) if KIND[k] != SPLIT_V]
IN_PSUM = [k for k in range(BLOCKS) if KIND[k] == SPLIT_V]
SPLIT = [k for k in range(BLOCKS) if KIND[k] in (SPLIT_G, SPLIT_V)]
BY_G = [k for k in range(BLOCKS) if KIND[k] == SPLIT_G]
PLAIN = [k for k in range(BLOCKS) if KIND[k] == WHOLE]
T_SLOTS = 8
V_SLOTS = 4
S_SLOTS = 6
LAG = 3
V_LOW = 3
FIRST = min(range(BLOCKS), key=lambda k: k + (-0.5 if k in PLAIN else LAG))
LAST = max(range(BLOCKS), key=lambda k: k + (-0.5 if k in PLAIN else LAG))

ROWS = 512
FULL = N // ROWS
NARROW = -(-(N - FULL * ROWS) // SQ) * SQ
NARROW_AT = N - NARROW
DOUBLE = FULL * ROWS - NARROW_AT
PAIRS = (FULL - 1) // 2

A_RELU, PE_TURN_OUT, V_RESIDUAL, V_STATS, V_VAR, A_ROOT, V_RSTD, V_SHIFT, A_NORM, A_STORE, A_STORED = \
    10, 11, 22, 23, 26, 30, 32, 33, 36, 38, 58
PE_TURN_X, A_MOVE_X, PE_ADD_X = 50, 60, 66
A_REST_HI, V_REST_LO = 70, 74
SKEW = 60


def chunk_of(k):
    return next(c for c in range(CHUNKS) if k < CHUNK_AT[c + 1] or c == CHUNKS - 1)


def chunk_end(c):
    return BLOCKS if c == CHUNKS - 1 else CHUNK_AT[c + 1]


def seg_of(c):
    return SQ * CHUNK_BLOCKS[c] + (REST_SEG if c == CHUNKS - 1 else 0)


def col_of(c, a):
    return CHUNK_AT[c] * P + a * seg_of(c)


def slot(among, slots, k):
    return among.index(k) % slots


def done(t, among, k):
    return len(among) * t + among.index(k) + 1


def before(t, among, slots, k):
    n = among.index(k) - slots
    if n >= 0:
        return t, among[n]
    return t - 1, [b for b in among if slot(among, slots, b) == slot(among, slots, k)][-1]


def segments(rows):
    return [(q, min(P, rows - q * P)) for q in range(-(-rows // P))]


def wait(eng, semaphore, count):
    if not isinstance(count, int) or count > 0:
        eng.wait_ge(semaphore, count)


def build(nc, x, adj, item, w_item, b_item, w_user, b_user, out):
    ctx = ExitStack()
    with ctx:
        def sb(name, shape, dtype=FP32):
            return ctx.enter_context(nc.sbuf_tensor(name, shape, dtype))

        def ps(name, shape):
            return ctx.enter_context(nc.psum_tensor(name, shape, FP32))

        def sem(name):
            return ctx.enter_context(nc.semaphore(name))

        h = sb("h", [P, len(PLAIN), D])
        h_hi = sb("h_hi", [P, len(SPLIT), D], FP32R)
        h_lo = sb("h_lo", [P, len(SPLIT), D], FP32R)
        raw = [sb(f"raw{i}", [P, ROWS // SQ, RAW_COLS[i]]) for i in range(RAW)]
        adjT = sb("adjT", [P, T_SLOTS, ROWS])
        adj_hi = sb("adj_hi", [P, S_SLOTS, ROWS], FP32R)
        adj_lo = sb("adj_lo", [P, S_SLOTS, ROWS], FP32R)
        ident = sb("ident", [P, P])
        h_rest = sb("h_rest", [P, D], FP32R)
        adj_rest = sb("adj_rest", [P, ROWS], FP32R)
        w_itemT = sb("w_itemT", [P, D])
        w_userT = sb("w_userT", [P, D])
        b_item_row = sb("b_item_row", [P, D])
        b_user_col = sb("b_user_col", [P, 1])
        eps_col = sb("eps_col", [P, 1])
        item_rest = sb("item_rest", [P, D])
        x_nat = sb("x_nat", [P, 2, ROWS // P, D])
        xT = sb("xT", [P, ROWS])
        act_out = sb("act_out", [P, ROWS])
        y = sb("y", [P, ROWS // P, D])
        stats = sb("stats", [P, ROWS // P, 6])
        mv = sb("mv", [P, ROWS // P, 2])
        std = sb("std", [P, ROWS // P])
        neg_mean = sb("neg_mean", [P, ROWS // P])
        rstd = sb("rstd", [P, ROWS // P])
        shift = sb("shift", [P, ROWS // P])
        o = sb("o", [P, 2, ROWS // P, D])
        stage = [raw[RAW - 1][:, :, :].rearrange("p r c -> p (r c)").rearrange("p (b d) -> p b d", d=D),
                 adjT[:, :, :].rearrange("p s (b d) -> p (s b) d", d=D)]
        STAGE = ROWS // SQ * RAW_COLS[RAW - 1] // D
        assert BLOCKS - 1 - STAGE <= T_SLOTS * ROWS // D
        STAGED_U = -(-STAGE // U)
        w_raw = y[:, 0:2, :]
        itemT = act_out[:, :].rearrange("p (s u d) -> p s u d", s=2, u=U)
        rest_sum, rest_low = y[:, 2, :], y[:, 3, :]
        H_SLOTS = 2 * ROWS // D // U
        h_sum = o[:, :, :, :].rearrange("p g (s u) d -> p (g s) u d", u=U)

        acc = [ps(f"acc{i}", [P, ROWS]) for i in range(2)]
        adjT_ps = ps("adjT_ps", [P, V_SLOTS, ROWS])
        ps_x = ps("ps_x", [P, ROWS])
        ps_o = ps("ps_o", [P, ROWS // P, D])
        ps_t = [adjT_ps[:, i, 0:U * D].rearrange("p (u d) -> p u d", u=U) for i in range(2)]
        ps_h = [adjT_ps[:, 2 + i, 0:U * D].rearrange("p (u d) -> p u d", u=U) for i in range(2)]

        ident_zero = sem("ident_zero")
        ident_ready = sem("ident_ready")
        w_loaded = sem("w_loaded")
        bias_loaded = sem("bias_loaded")
        rest_zeroed = sem("rest_zeroed")
        rest_masks = sem("rest_masks")
        h_rest_rounded = sem("h_rest_rounded")
        h_rest_lo = sem("h_rest_lo")
        h_rest_ready = sem("h_rest_ready")
        rest_hi = sem("rest_hi")
        rest_lo = sem("rest_lo")
        rest_ready = sem("rest_ready")
        item_loaded = [sem(f"item_loaded{c}") for c in range(CHUNKS)]
        item_rest_loaded = sem("item_rest_loaded")
        w_turned = sem("w_turned")
        w_ready = sem("w_ready")
        item_turned = sem("item_turned")
        itemT_ready = sem("itemT_ready")
        h_product = sem("h_product")
        h_sum_ready = sem("h_sum_ready")
        h_hi_ready = sem("h_hi_ready")
        h_lo_ready = sem("h_lo_ready")
        consts_set = sem("consts_set")
        pad_zeroed = sem("pad_zeroed")
        raw_loaded = [sem(f"raw_loaded{i}") for i in range(RAW)]
        turned = sem("turned")
        hi_ready = sem("hi_ready")
        lo_ready_g = sem("lo_ready_g")
        lo_ready_v = sem("lo_ready_v")
        whole_used = sem("whole_used")
        rest_used = sem("rest_used")
        split_used = sem("split_used")
        x_loaded = [sem(f"x_loaded{i}") for i in range(2)]
        x_turned = sem("x_turned")
        xT_ready = sem("xT_ready")
        x_done = sem("x_done")
        relu_done = sem("relu_done")
        out_turned = sem("out_turned")
        y_ready = sem("y_ready")
        stats_ready = sem("stats_ready")
        var_ready = sem("var_ready")
        std_ready = sem("std_ready")
        rstd_ready = sem("rstd_ready")
        shift_ready = sem("shift_ready")
        o_ready = sem("o_ready")
        out_stored = [sem(f"out_stored{i}") for i in range(2)]

        rest_at = SQ * CHUNK_BLOCKS[CHUNKS - 1]
        raw_rest = raw[RAW - 1][:, :, rest_at:rest_at + REST_SEG]
        raw_rest_hi, raw_rest_lo = (raw[RAW - 1][:, :, rest_at + n * REST_SEG:rest_at + (n + 2) * REST_SEG]
                                    for n in (1, 3))
        rest_w = sb("rest_w", [P, 2])

        def pieces(c):
            lo, hi = CHUNK_AT[c], CHUNK_AT[c + 1]
            mid = min(max(STAGE, lo), hi)
            return [(s, b - s * STAGE, b - lo, n) for s, b, n in ((0, lo, mid - lo), (1, mid, hi - mid)) if n]

        def loads_of(c):
            return 16 * QUADS * len(pieces(c))

        block = ctx.enter_context(nc.Block())

        @block.sync
        def _(sp):
            def load_chunk(t, row0, rows, c):
                if c >= RAW:
                    wait(sp, turned, BLOCKS * t + chunk_end(c - RAW))
                else:
                    wait(sp, turned, BLOCKS * (t - 1) + chunk_end(c + RAW))
                for a in range(QUADS):
                    src = adj[bass.ds(row0, rows), col_of(c, a):col_of(c, a) + seg_of(c)]
                    sp.dma_start(raw[c % RAW][SQ * a:SQ * a + SQ, 0:rows // SQ, 0:seg_of(c)],
                                 src.rearrange("(r i) c -> i r c", i=SQ)).then_inc(raw_loaded[c % RAW], 16)

            def load_x(par, row0):
                sp.dma_start(x_nat[:, par, :, :],
                             x[bass.ds(row0, ROWS), :].rearrange("(q p) d -> p q d", p=P)
                             ).then_inc(x_loaded[par], 16)

            def load_items(c):
                for s, at, b0, n in pieces(c):
                    for a in range(QUADS):
                        first = col_of(c, a) + SQ * b0
                        sp.dma_start(stage[s][SQ * a:SQ * a + SQ, at:at + n, :],
                                      item[first:first + SQ * n, :].rearrange("(b j) d -> j b d", j=SQ)
                                      ).then_inc(item_loaded[c], 16)

            sp.dma_start(w_raw[:, 0, :], w_item).then_inc(w_loaded, 16)
            sp.dma_start(w_raw[:, 1, :], w_user).then_inc(w_loaded, 16)
            load_items(0)
            sp.dma_start(b_item_row[:, :], b_item.rearrange("(o d) -> o d", o=1).to_broadcast([P, D])
                         ).then_inc(bias_loaded, 16)
            sp.dma_start(b_user_col[:, :], b_user.rearrange("(d o) -> d o", o=1)).then_inc(bias_loaded, 16)
            for c in range(1, CHUNKS):
                load_items(c)
            sp.wait_ge(rest_zeroed, 1)
            for a in range(QUADS):
                first = col_of(CHUNKS - 1, a) + seg_of(CHUNKS - 1) - REST_SEG
                sp.dma_start(item_rest[SQ * a:SQ * a + REST_SEG, :], item[first:first + REST_SEG, :]
                             ).then_inc(item_rest_loaded, 16)
            for c in range(RAW):
                if c == RAW - 1:
                    sp.wait_ge(pad_zeroed, 1)
                load_chunk(0, 0, ROWS, c)
            load_x(0, 0)
            with sp.Fori(0, PAIRS) as i:
                for par in range(2):
                    t = 2 * i + par
                    for c in range(RAW, CHUNKS):
                        load_chunk(t, ROWS * t, ROWS, c)
                    for c in range(RAW):
                        load_chunk(t + 1, ROWS * t + ROWS, ROWS, c)
                    load_x(1 - par, ROWS * t + ROWS)
            for c in range(RAW, CHUNKS):
                load_chunk(FULL - 1, ROWS * (FULL - 1), ROWS, c)
            for c in range(RAW):
                load_chunk(FULL, NARROW_AT, NARROW, c)
            for q, rows in segments(NARROW):
                sp.dma_start(x_nat[0:rows, FULL % 2, q, :],
                             x[NARROW_AT + P * q:NARROW_AT + P * q + rows, :]).then_inc(x_loaded[FULL % 2], 16)
            for c in range(RAW, CHUNKS):
                load_chunk(FULL, NARROW_AT, NARROW, c)

        @block.gpsimd
        def _(pool):
            nc.gpsimd.memset(ident[:, :], 0.0).then_inc(ident_zero, 1)
            pool.wait_ge(ident_zero, 1)
            nc.gpsimd.affine_select(out=ident[:, :], in_=ident[:, :], compare_op=ALU.not_equal, fill=1.0,
                                    base=0, pattern=[[-1, P]], channel_multiplier=1).then_inc(ident_ready, 1)

            def blocks(t, k0, k1, rows=ROWS):
                for k in range(k0, k1):
                    if KIND[k] == SPLIT_G:
                        pool.wait_ge(hi_ready, done(t, SPLIT, k))
                        s = slot(SPLIT, S_SLOTS, k)
                        nc.gpsimd.tensor_tensor(adj_lo[:, s, 0:rows], adjT[:, slot(IN_SBUF, T_SLOTS, k), 0:rows],
                                                adj_hi[:, s, 0:rows].bitcast(FP32), ALU.subtract
                                                ).then_inc(lo_ready_g, 1)

            for n in range(len(SPLIT) // U):
                pool.wait_ge(h_hi_ready, n + 1)
                nc.gpsimd.tensor_tensor(h_lo[:, U * n:U * n + U, :], h_sum[:, n % H_SLOTS, :, :],
                                        h_hi[:, U * n:U * n + U, :].bitcast(FP32), ALU.subtract
                                        ).then_inc(h_lo_ready, 1)

            blocks(0, 0, SKEW)
            with pool.Fori(0, FULL - 1) as t:
                blocks(t, SKEW, BLOCKS)
                blocks(t + 1, 0, SKEW)
            blocks(FULL - 1, SKEW, BLOCKS)
            blocks(FULL, 0, BLOCKS, NARROW)

        @block.tensor
        def _(pe):
            def blocks(i, par, k0, k1, rows=ROWS, last_out=True):
                t = 2 * i + par
                for k in range(k0, k1):
                    if k == PE_TURN_OUT and last_out:
                        turn_out(t - 1, ROWS)
                    if k == PE_TURN_X:
                        pe.wait_ge(x_loaded[par], 16 * i + 16 * (1 if rows == ROWS else len(segments(rows))))
                        for q, n in segments(rows):
                            last = nc.tensor.transpose(ps_x[:, P * q:P * q + n], x_nat[0:n, par, q, :],
                                                       ident[0:n, 0:n])
                        last.then_inc(x_turned, 1)
                    if k == PE_ADD_X:
                        pe.wait_ge(xT_ready, t + 1)
                        nc.tensor.matmul(acc[par][:, 0:rows], w_userT[:, :], xT[:, 0:rows],
                                         start=False, stop=False).then_inc(x_done, 1)
                    if KIND[k] == WHOLE:
                        pe.wait_ge(turned, BLOCKS * t + k + 1)
                        nc.tensor.matmul(acc[par][:, 0:rows], h[:, PLAIN.index(k), :],
                                         adjT[:, slot(IN_SBUF, T_SLOTS, k), 0:rows],
                                         start=(k == FIRST), stop=(k == LAST)).then_inc(whole_used, 1)
                    if k >= LAG:
                        split_block(t, par, k - LAG, rows)
                    elif last_out:
                        split_block(t - 1, 1 - par, k - LAG + BLOCKS, ROWS)

            def split_block(t, par, k, rows):
                if KIND[k] == REST_BLOCK:
                    pe.wait_ge(rest_ready, t + 1)
                    nc.tensor.matmul(acc[par][:, 0:rows], h_rest[:, :], adj_rest[:, 0:rows],
                                     start=False, stop=(k == LAST)).then_inc(rest_used, 1)
                if k not in SPLIT:
                    return
                if KIND[k] == SPLIT_G:
                    pe.wait_ge(lo_ready_g, done(t, BY_G, k))
                else:
                    pe.wait_ge(lo_ready_v, done(t, IN_PSUM, k))
                n, s = SPLIT.index(k), slot(SPLIT, S_SLOTS, k)
                for part, (a, w) in enumerate(((adj_hi, h_hi), (adj_hi, h_lo), (adj_lo, h_hi))):
                    last = nc.tensor.matmul(acc[par][:, 0:rows], w[:, n, :], a[:, s, 0:rows],
                                            start=(k == FIRST and part == 0), stop=(k == LAST and part == 2))
                last.then_inc(split_used, 1)

            def turn_out(t, rows):
                pe.wait_ge(relu_done, t + 1)
                for q, n in segments(rows):
                    last = nc.tensor.transpose(ps_o[0:n, q, :], act_out[:, P * q:P * q + n], ident[:, :])
                last.then_inc(out_turned, 1)

            pe.wait_ge(ident_ready, 1)
            pe.wait_ge(w_loaded, 32)
            for n in range(2):
                last = nc.tensor.transpose(ps_t[1][:, n, :], w_raw[:, n, :], ident[:, :])
            last.then_inc(w_turned, 1)

            def turn_items(u):
                c = chunk_of(U * u)
                pe.wait_ge(item_loaded[c], loads_of(c))
                if u == 1:
                    pe.wait_ge(w_ready, 1)
                wait(pe, itemT_ready, u - 1)
                for j, k in enumerate(range(U * u, min(U * u + U, BLOCKS))):
                    if k == BLOCKS - 1:
                        pe.wait_ge(item_rest_loaded, 16 * QUADS)
                        src = item_rest[:, :]
                    else:
                        src = stage[k // STAGE][:, k % STAGE, :]
                    last = nc.tensor.transpose(ps_t[u % 2][:, j, :], src, ident[:, :])
                last.then_inc(item_turned, 1)

            turn_items(0)
            turn_items(1)
            for u in range(UNITS):
                pe.wait_ge(itemT_ready, u + 1)
                wait(pe, h_sum_ready, u - 1)
                for j, k in enumerate(range(U * u, min(U * u + U, BLOCKS))):
                    last = nc.tensor.matmul(ps_h[u % 2][:, j, :], itemT[:, u % 2, j, :], w_itemT[:, :],
                                            start=True, stop=True)
                last.then_inc(h_product, 1)
                if u + 2 < UNITS:
                    turn_items(u + 2)
            pe.wait_ge(h_lo_ready, len(SPLIT) // U)
            pe.wait_ge(h_sum_ready, UNITS)

            blocks(0, 0, 0, SKEW, last_out=False)
            pe.wait_ge(h_rest_ready, 1)
            with pe.Fori(0, PAIRS) as i:
                blocks(i, 0, SKEW, BLOCKS)
                blocks(i, 1, 0, SKEW)
                blocks(i, 1, SKEW, BLOCKS)
                blocks(i + 1, 0, 0, SKEW)
            blocks(PAIRS, 0, SKEW, BLOCKS)
            blocks(PAIRS, 1, 0, BLOCKS, NARROW)
            for k in range(BLOCKS - LAG, BLOCKS):
                split_block(FULL, 1, k, NARROW)
            turn_out(FULL, NARROW)

        @block.scalar
        def _(act):
            def blocks(i, par, k0, k1, rows=ROWS, last_out=True):
                t = 2 * i + par
                for k in range(k0, k1):
                    if last_out:
                        finish(k, i if par == 1 else i - 1, 1 - par)
                    if k == A_MOVE_X:
                        act.wait_ge(x_turned, t + 1)
                        nc.scalar.copy(xT[:, 0:rows], ps_x[:, 0:rows]).then_inc(xT_ready, 1)
                    if k == A_REST_HI:
                        act.wait_ge(raw_loaded[RAW - 1], 16 * QUADS * (CHUNKS // RAW) * (t + 1))
                        r = rows // SQ
                        nc.scalar.copy(
                            raw_rest_hi[:, 0:r, :].rearrange("p r (n j) -> p r n j", n=2).bitcast(FP32R),
                            raw_rest[:, 0:r, :].rearrange("p r (n j) -> p r n j", n=1).to_broadcast(
                                [P, r, 2, REST_SEG])).then_inc(rest_hi, 1)
                    if KIND[k] == REST_BLOCK:
                        act.wait_ge(turned, BLOCKS * t + k + 1)
                        nc.scalar.copy(adj_rest[:, 0:rows], adjT[:, slot(IN_SBUF, T_SLOTS, k), 0:rows]
                                       ).then_inc(rest_ready, 1)
                    if k not in SPLIT:
                        continue
                    act.wait_ge(turned, BLOCKS * t + k + 1)
                    bt, bk = before(t, SPLIT, S_SLOTS, k)
                    wait(act, split_used, done(bt, SPLIT, bk))
                    if KIND[k] == SPLIT_G:
                        src = adjT[:, slot(IN_SBUF, T_SLOTS, k), 0:rows]
                    else:
                        src = adjT_ps[:, slot(IN_PSUM, V_SLOTS, k), 0:rows]
                    nc.scalar.copy(adj_hi[:, slot(SPLIT, S_SLOTS, k), 0:rows], src).then_inc(hi_ready, 1)

            def finish(k, i, par):
                t = 2 * i + par
                if k == A_RELU:
                    relu(t, par, ROWS)
                if k == A_ROOT:
                    root(t)
                if k == A_NORM:
                    norm(t, par, ROWS)
                if k == A_STORE:
                    act.wait_ge(o_ready, t + 1)
                    act.dma_start(out[bass.ds(ROWS * t, ROWS), :].rearrange("(q p) d -> p q d", p=P),
                                  o[:, par, :, :]).then_inc(out_stored[par], 16)
                if k == A_STORED:
                    act.wait_ge(out_stored[par], 16 * i + 16)

            def relu(t, par, rows):
                act.wait_ge(split_used, len(SPLIT) * (t + 1))
                act.wait_ge(whole_used, len(PLAIN) * (t + 1))
                act.wait_ge(rest_used, t + 1)
                act.wait_ge(x_done, t + 1)
                nc.scalar.activation(act_out[:, 0:rows], acc[par][:, 0:rows], ACT.Relu,
                                     bias=b_user_col[:, 0:1]).then_inc(relu_done, 1)

            def root(t):
                act.wait_ge(var_ready, t + 1)
                nc.scalar.activation(std[:, :], mv[:, :, 1], ACT.Sqrt, bias=eps_col[:, 0:1])
                nc.scalar.mul(neg_mean[:, :], mv[:, :, 0], -1.0).then_inc(std_ready, 1)

            def norm(t, par, rows):
                act.wait_ge(shift_ready, t + 1)
                for q, n in segments(rows):
                    last = nc.scalar.activation(o[0:n, par, q, :], y[0:n, q, :], ACT.Identity,
                                                bias=shift[0:n, q:q + 1], scale=rstd[0:n, q:q + 1])
                last.then_inc(o_ready, 1)

            act.wait_ge(w_turned, 1)
            nc.scalar.copy(w_itemT[:, :], ps_t[1][:, 0, :])
            nc.scalar.copy(w_userT[:, :], ps_t[1][:, 1, :]).then_inc(w_ready, 1)
            for u in range(UNITS):
                if U * u in SPLIT:
                    n = SPLIT.index(U * u)
                    act.wait_ge(h_sum_ready, u + 1)
                    nc.scalar.copy(h_hi[:, n:n + U, :], h_sum[:, n // U % H_SLOTS, :, :]).then_inc(h_hi_ready, 1)
            act.wait_ge(bias_loaded, 32)
            act.wait_ge(consts_set, 1)
            act.wait_ge(h_sum_ready, UNITS)
            nc.scalar.copy(h_rest[:, :], rest_sum).then_inc(h_rest_rounded, 1)

            blocks(0, 0, 0, SKEW, last_out=False)
            with act.Fori(0, PAIRS) as i:
                blocks(i, 0, SKEW, BLOCKS)
                blocks(i, 1, 0, SKEW)
                blocks(i, 1, SKEW, BLOCKS)
                blocks(i + 1, 0, 0, SKEW)
            blocks(PAIRS, 0, SKEW, BLOCKS)
            blocks(PAIRS, 1, 0, BLOCKS, NARROW)
            relu(FULL, 1, NARROW)
            root(FULL)
            norm(FULL, 1, NARROW)
            act.wait_ge(o_ready, FULL + 1)
            for q, n in segments(NARROW):
                lo = DOUBLE if q == 0 else 0
                act.dma_start(out[NARROW_AT + P * q + lo:NARROW_AT + P * q + n, :], o[lo:n, 1, q, :]
                              ).then_inc(out_stored[1], 16)
            act.wait_ge(out_stored[0], 16 * (PAIRS + 1))
            act.wait_ge(out_stored[1], 16 * PAIRS + 16 * len(segments(NARROW)))

        @block.vector
        def _(dve):
            def blocks(i, par, k0, k1, rows=ROWS, last_out=True):
                t = 2 * i + par
                for k in range(k0, k1):
                    c = chunk_of(k)
                    if last_out:
                        finish(k, i if par == 1 else i - 1, 1 - par, ROWS)
                    if k == CHUNK_AT[c]:
                        fills = CHUNKS // RAW * t + c // RAW + 1
                        dve.wait_ge(raw_loaded[c % RAW], 16 * QUADS * fills)
                    if k == V_VAR and last_out:
                        dve.wait_ge(stats_ready, t)
                    if k == V_REST_LO:
                        dve.wait_ge(rest_hi, t + 1)
                        r = rows // SQ
                        nc.vector.tensor_tensor(
                            raw_rest_lo[:, 0:r, :].rearrange("p r (n j) -> p r n j", n=2),
                            raw_rest[:, 0:r, :].rearrange("p r (n j) -> p r n j", n=1).to_broadcast(
                                [P, r, 2, REST_SEG]),
                            raw_rest_hi[:, 0:r, :].rearrange("p r (n j) -> p r n j", n=2),
                            ALU.subtract).then_inc(rest_lo, 1)
                    if KIND[k] == REST_BLOCK:
                        dve.wait_ge(rest_lo, t + 1)
                    if k % U == 0:
                        turn(t, k, min(U, BLOCKS - k), rows)
                    if k == V_VAR and last_out:
                        variance(ROWS)
                    if k >= V_LOW and KIND[k - V_LOW] == SPLIT_V:
                        low(t, k - V_LOW, rows)

            def turn(t, k, n, rows):
                for b in range(k, k + n):
                    if KIND[b] == SPLIT_V:
                        bt, bk = before(t, IN_PSUM, V_SLOTS, b)
                        wait(dve, lo_ready_v, done(bt, IN_PSUM, bk))
                    elif KIND[before(t, IN_SBUF, T_SLOTS, b)[1]] == REST_BLOCK:
                        wait(dve, rest_ready, before(t, IN_SBUF, T_SLOTS, b)[0] + 1)
                    elif KIND[before(t, IN_SBUF, T_SLOTS, b)[1]] == SPLIT_G:
                        bt, bk = before(t, IN_SBUF, T_SLOTS, b)
                        wait(dve, lo_ready_g, done(bt, BY_G, bk))
                    else:
                        bt, bk = before(t, IN_SBUF, T_SLOTS, b)
                        wait(dve, whole_used, done(bt, PLAIN, bk))
                if KIND[k] == SPLIT_V:
                    s = slot(IN_PSUM, V_SLOTS, k)
                    dst = adjT_ps[:, s:s + n, 0:rows]
                else:
                    s = slot(IN_SBUF, T_SLOTS, k)
                    dst = adjT[:, s:s + n, 0:rows]
                c = chunk_of(k)
                col = SQ * (k - CHUNK_AT[c])
                src = raw[c % RAW][:, 0:rows // SQ, col:col + SQ * n].rearrange("p r (b j) -> p b r j", j=SQ)
                nc.vector.transpose(dst.rearrange("p b (r i) -> p b r i", i=SQ), src).then_inc(turned, n)

            def low(t, k, rows):
                dve.wait_ge(hi_ready, done(t, SPLIT, k))
                s, v = slot(SPLIT, S_SLOTS, k), slot(IN_PSUM, V_SLOTS, k)
                nc.vector.tensor_tensor(adj_lo[:, s, 0:rows], adjT_ps[:, v, 0:rows],
                                        adj_hi[:, s, 0:rows].bitcast(FP32), ALU.subtract).then_inc(lo_ready_v, 1)

            def variance(rows):
                for q, n in segments(rows):
                    last = nc.vector.bn_aggr(mv[0:n, q, :], stats[0:n, q, :])
                last.then_inc(var_ready, 1)

            def finish(k, i, par, rows):
                t = 2 * i + par
                if k == V_RESIDUAL:
                    dve.wait_ge(out_turned, t + 1)
                    for q, m, n in [(0, rows // P, P), (rows // P, 1, rows % P)]:
                        if n:
                            last = nc.vector.tensor_tensor(y[0:n, q:q + m, :], ps_o[0:n, q:q + m, :],
                                                           x_nat[0:n, par, q:q + m, :], ALU.add)
                    last.then_inc(y_ready, 1)
                if k == V_STATS:
                    dve.wait_ge(y_ready, t + 1)
                    for q, n in segments(rows):
                        last = nc.vector.bn_stats(stats[0:n, q, :], y[0:n, q, :])
                    last.then_inc(stats_ready, 1)
                if k == V_RSTD:
                    dve.wait_ge(std_ready, t + 1)
                    nc.vector.reciprocal(rstd[:, :], std[:, :]).then_inc(rstd_ready, 1)
                if k == V_SHIFT:
                    dve.wait_ge(rstd_ready, t + 1)
                    nc.vector.tensor_tensor(shift[:, :], neg_mean[:, :], rstd[:, :], ALU.mult).then_inc(shift_ready, 1)

            nc.vector.memset(item_rest[:, :], 0.0).then_inc(rest_zeroed, 1)
            nc.vector.memset(eps_col[:, :], EPS).then_inc(consts_set, 1)

            dve.wait_ge(ident_ready, 1)
            marks = ident[:, :].rearrange("p (a q) -> p a q", q=SQ)[:, :, REST_SEG:REST_COPIES * REST_SEG]
            marks = marks.rearrange("p a (n s j) -> p a n s j", s=2, j=REST_SEG)
            for n in range(2):
                last = nc.vector.reduce_sum(rest_w[:, n:n + 1], marks[:, :, :, n, :], axis=mybir.AxisListType.XYZ)
            last.then_inc(rest_masks, 1)

            def move_items(u):
                n = min(U, BLOCKS - U * u)
                dve.wait_ge(item_turned, u + 1)
                wait(dve, h_product, u - 1)
                if u < UNITS - 1:
                    nc.vector.tensor_copy(itemT[:, u % 2, 0:n, :], ps_t[u % 2][:, 0:n, :]).then_inc(itemT_ready, 1)
                    return
                dst, src = (m.rearrange("p (a q) -> p a q", q=SQ) for m in (itemT[:, u % 2, 0, :], ps_t[u % 2][:, 0, :]))
                nc.vector.tensor_copy(dst[:, :, REST_COPIES * REST_SEG:], src[:, :, REST_COPIES * REST_SEG:])
                nc.vector.tensor_copy(
                    dst[:, :, 0:REST_COPIES * REST_SEG].rearrange("p a (n j) -> p a n j", j=REST_SEG),
                    src[:, :, 0:REST_SEG].rearrange("p a (n j) -> p a n j", n=1).to_broadcast(
                        [P, QUADS, REST_COPIES, REST_SEG])).then_inc(itemT_ready, 1)

            move_items(0)
            move_items(1)
            dve.wait_ge(bias_loaded, 32)
            for u in range(UNITS):
                n = min(U, BLOCKS - U * u)
                dve.wait_ge(h_product, u + 1)
                if u == UNITS - 1:
                    dst = rest_sum.rearrange("p (n d) -> p n d", n=1)
                elif U * u in SPLIT:
                    m = SPLIT.index(U * u) // U
                    wait(dve, h_lo_ready, m - H_SLOTS + 1)
                    dst = h_sum[:, m % H_SLOTS, :, :]
                else:
                    dst = h[:, PLAIN.index(U * u):PLAIN.index(U * u) + n, :]
                nc.vector.tensor_tensor(dst, ps_h[u % 2][:, 0:n, :],
                                        b_item_row[:, :].rearrange("p (o d) -> p o d", o=1).to_broadcast([P, n, D]),
                                        ALU.add).then_inc(h_sum_ready, 1)
                if u + 2 < UNITS:
                    move_items(u + 2)
                if u + 3 == STAGED_U:
                    nc.vector.memset(raw[RAW - 1][:, :, SQ * CHUNK_BLOCKS[RAW - 1]:], 0.0).then_inc(pad_zeroed, 1)

            blocks(0, 0, 0, T_SLOTS, last_out=False)
            dve.wait_ge(h_rest_rounded, 1)
            nc.vector.tensor_tensor(rest_low, rest_sum, h_rest[:, :].bitcast(FP32), ALU.subtract).then_inc(h_rest_lo, 1)
            dve.wait_ge(h_rest_lo, 1)
            dve.wait_ge(rest_masks, 1)
            nc.vector.tensor_scalar(rest_low, rest_low, rest_w[:, 1:2], None, ALU.mult).then_inc(h_rest_lo, 1)
            dve.wait_ge(h_rest_lo, 2)
            nc.vector.scalar_tensor_tensor(out=h_rest[:, :], in0=h_rest[:, :].bitcast(FP32), scalar=rest_w[:, 0:1],
                                           in1=rest_low, op0=ALU.mult, op1=ALU.add).then_inc(h_rest_ready, 1)
            blocks(0, 0, T_SLOTS, SKEW, last_out=False)
            with dve.Fori(0, PAIRS) as i:
                blocks(i, 0, SKEW, BLOCKS)
                blocks(i, 1, 0, SKEW)
                blocks(i, 1, SKEW, BLOCKS)
                blocks(i + 1, 0, 0, SKEW)
            blocks(PAIRS, 0, SKEW, BLOCKS)
            blocks(PAIRS, 1, 0, BLOCKS, NARROW)
            finish(V_RESIDUAL, PAIRS, 1, NARROW)
            finish(V_STATS, PAIRS, 1, NARROW)
            dve.wait_ge(stats_ready, FULL + 1)
            variance(NARROW)
            finish(V_RSTD, PAIRS, 1, NARROW)
            finish(V_SHIFT, PAIRS, 1, NARROW)


_INS = ["x", "adj", "L0_gnn_item_feat", "L0_gnn_W_item", "L0_gnn_b_item", "L0_gnn_W_user", "L0_gnn_b_user"]


def kernel(**inputs):
    import numpy as _np
    import concourse.bacc as _bacc
    from concourse import mybir as _mybir
    from concourse.bass_utils import run_bass_kernel_spmd as _run

    nc = _bacc.Bacc("TRN2", target_bir_lowering=False, num_devices=1)
    arrays, args = {}, []
    for name in _INS:
        a = _np.ascontiguousarray(inputs[name])
        arrays[f"in_{name}_dram"] = a
        args.append(nc.dram_tensor(f"in_{name}_dram", a.shape, _mybir.dt.from_np(a.dtype), kind="ExternalInput").ap())
    args.append(nc.dram_tensor("out_0_dram", (N, D), _mybir.dt.float32, kind="ExternalOutput").ap())
    build(nc, *args)
    return _run(nc, [arrays], core_ids=[0]).results[0]["out_0_dram"]
```
